# Optimizing a Trainium2 kernel written in Bass

```python
import numpy as np
import jax
import jax.numpy as jnp

def _softmax(x, axis=-1):
    return jax.nn.softmax(x, axis=axis)

def _gelu(x):
    return jax.nn.gelu(x, approximate=True)

def _silu(x):
    return jax.nn.silu(x)

def _sigmoid(x):
    return jax.nn.sigmoid(x)

def _layernorm(x, axis=-1, eps=1e-05):
    m = jnp.mean(x, axis=axis, keepdims=True)
    v = jnp.var(x, axis=axis, keepdims=True)
    return (x - m) / jnp.sqrt(v + eps)

def _scatter_add(tgt, idx, src, axis=0):
    return tgt.at[idx].add(src)

def _segment_sum(src, seg, n):
    return jax.ops.segment_sum(src, seg, n)
kernel_name = 'mk_dlrm_tower_d1_rec_r8_44a446'

def setup_inputs(seed: int=0):
    np.random.seed(seed)
    _w = jnp.asarray

    def _rec_inputs():
        import jax
        import jax.numpy as jnp
        _tk = jax.random.key(seed)
        ids = jnp.stack([jax.random.randint(jax.random.fold_in(_tk, 200 + f), (512,), 0, v, jnp.int32) for f, v in enumerate([1250, 125000, 12500, 12500, 1250, 1250, 1000, 1250, 1250, 12500, 12500, 1000, 12500, 1000, 1000, 1250, 1250, 1000, 1250, 1250, 12500, 1000, 12500, 1250, 12500, 1250, 1000])], axis=1)
        tbl_0 = 0.05 * jax.random.normal(jax.random.fold_in(_tk, 500 + 0), (1250, 128), jnp.float32)
        tbl_1 = 0.05 * jax.random.normal(jax.random.fold_in(_tk, 500 + 1), (125000, 128), jnp.float32)
        tbl_2 = 0.05 * jax.random.normal(jax.random.fold_in(_tk, 500 + 2), (12500, 128), jnp.float32)
        tbl_3 = 0.05 * jax.random.normal(jax.random.fold_in(_tk, 500 + 3), (12500, 128), jnp.float32)
        tbl_4 = 0.05 * jax.random.normal(jax.random.fold_in(_tk, 500 + 4), (1250, 128), jnp.float32)
        tbl_5 = 0.05 * jax.random.normal(jax.random.fold_in(_tk, 500 + 5), (1250, 128), jnp.float32)
        tbl_6 = 0.05 * jax.random.normal(jax.random.fold_in(_tk, 500 + 6), (1000, 128), jnp.float32)
        tbl_7 = 0.05 * jax.random.normal(jax.random.fold_in(_tk, 500 + 7), (1250, 128), jnp.float32)
        tbl_8 = 0.05 * jax.random.normal(jax.random.fold_in(_tk, 500 + 8), (1250, 128), jnp.float32)
        tbl_9 = 0.05 * jax.random.normal(jax.random.fold_in(_tk, 500 + 9), (12500, 128), jnp.float32)
        tbl_10 = 0.05 * jax.random.normal(jax.random.fold_in(_tk, 500 + 10), (12500, 128), jnp.float32)
        tbl_11 = 0.05 * jax.random.normal(jax.random.fold_in(_tk, 500 + 11), (1000, 128), jnp.float32)
        tbl_12 = 0.05 * jax.random.normal(jax.random.fold_in(_tk, 500 + 12), (12500, 128), jnp.float32)
        tbl_13 = 0.05 * jax.random.normal(jax.random.fold_in(_tk, 500 + 13), (1000, 128), jnp.float32)
        tbl_14 = 0.05 * jax.random.normal(jax.random.fold_in(_tk, 500 + 14), (1000, 128), jnp.float32)
        tbl_15 = 0.05 * jax.random.normal(jax.random.fold_in(_tk, 500 + 15), (1250, 128), jnp.float32)
        tbl_16 = 0.05 * jax.random.normal(jax.random.fold_in(_tk, 500 + 16), (1250, 128), jnp.float32)
        tbl_17 = 0.05 * jax.random.normal(jax.random.fold_in(_tk, 500 + 17), (1000, 128), jnp.float32)
        tbl_18 = 0.05 * jax.random.normal(jax.random.fold_in(_tk, 500 + 18), (1250, 128), jnp.float32)
        tbl_19 = 0.05 * jax.random.normal(jax.random.fold_in(_tk, 500 + 19), (1250, 128), jnp.float32)
        tbl_20 = 0.05 * jax.random.normal(jax.random.fold_in(_tk, 500 + 20), (12500, 128), jnp.float32)
        tbl_21 = 0.05 * jax.random.normal(jax.random.fold_in(_tk, 500 + 21), (1000, 128), jnp.float32)
        tbl_22 = 0.05 * jax.random.normal(jax.random.fold_in(_tk, 500 + 22), (12500, 128), jnp.float32)
        tbl_23 = 0.05 * jax.random.normal(jax.random.fold_in(_tk, 500 + 23), (1250, 128), jnp.float32)
        tbl_24 = 0.05 * jax.random.normal(jax.random.fold_in(_tk, 500 + 24), (12500, 128), jnp.float32)
        tbl_25 = 0.05 * jax.random.normal(jax.random.fold_in(_tk, 500 + 25), (1250, 128), jnp.float32)
        tbl_26 = 0.05 * jax.random.normal(jax.random.fold_in(_tk, 500 + 26), (1000, 128), jnp.float32)
        _rk = jax.random.fold_in(_tk, 7)
        r_bottom_mlp_out = 4.13588e-05 + 0.999923 * jax.random.normal(jax.random.fold_in(_rk, 101), (512, 128), jnp.float32)
        W_top1 = 0.0405887 * jax.random.normal(jax.random.fold_in(_tk, 801), (607, 512), jnp.float32)
        W_top2 = 0.0441942 * jax.random.normal(jax.random.fold_in(_tk, 802), (512, 256), jnp.float32)
        W_top3 = 0.0625 * jax.random.normal(jax.random.fold_in(_tk, 803), (256, 1), jnp.float32)
        b_top1 = jnp.zeros((512,), jnp.float32)
        b_top2 = jnp.zeros((256,), jnp.float32)
        return (r_bottom_mlp_out, ids, tbl_0, tbl_1, tbl_2, tbl_3, tbl_4, tbl_5, tbl_6, tbl_7, tbl_8, tbl_9, tbl_10, tbl_11, tbl_12, tbl_13, tbl_14, tbl_15, tbl_16, tbl_17, tbl_18, tbl_19, tbl_20, tbl_21, tbl_22, tbl_23, tbl_24, tbl_25, tbl_26, W_top1, b_top1, W_top2, b_top2, W_top3)
    r_bottom_mlp_out, ids, tbl_0, tbl_1, tbl_2, tbl_3, tbl_4, tbl_5, tbl_6, tbl_7, tbl_8, tbl_9, tbl_10, tbl_11, tbl_12, tbl_13, tbl_14, tbl_15, tbl_16, tbl_17, tbl_18, tbl_19, tbl_20, tbl_21, tbl_22, tbl_23, tbl_24, tbl_25, tbl_26, W_top1, b_top1, W_top2, b_top2, W_top3 = _rec_inputs()

    def _L0_rec_setup():
        import jax, jax.numpy as jnp
        import numpy as np
        NUM_FEATURES = 27

        def _tril_indices(F):
            idx = []
            for i in range(F):
                for j in range(i):
                    idx.append(i * F + j)
            return np.asarray(idx, dtype=np.int32)
        TRIL_IDX = _tril_indices(NUM_FEATURES)
        key = jax.random.key(seed)
        k1, k2 = jax.random.split(key)
        B, F, D = (8192, NUM_FEATURES, 128)
        features = jax.random.normal(k1, (B, F, D), dtype=jnp.float32)
        bottom_mlp_out = jax.random.normal(k2, (B, D), dtype=jnp.float32)
        return {'features': features, 'bottom_mlp_out': bottom_mlp_out}
    _L0_rec_all = _L0_rec_setup()
    _L0_rec_in = {k: v for k, v in _L0_rec_all.items() if k in ()}
    del _L0_rec_all
    return {'r_bottom_mlp_out': r_bottom_mlp_out, 'ids': ids, 'tbl_0': tbl_0, 'tbl_1': tbl_1, 'tbl_2': tbl_2, 'tbl_3': tbl_3, 'tbl_4': tbl_4, 'tbl_5': tbl_5, 'tbl_6': tbl_6, 'tbl_7': tbl_7, 'tbl_8': tbl_8, 'tbl_9': tbl_9, 'tbl_10': tbl_10, 'tbl_11': tbl_11, 'tbl_12': tbl_12, 'tbl_13': tbl_13, 'tbl_14': tbl_14, 'tbl_15': tbl_15, 'tbl_16': tbl_16, 'tbl_17': tbl_17, 'tbl_18': tbl_18, 'tbl_19': tbl_19, 'tbl_20': tbl_20, 'tbl_21': tbl_21, 'tbl_22': tbl_22, 'tbl_23': tbl_23, 'tbl_24': tbl_24, 'tbl_25': tbl_25, 'tbl_26': tbl_26, 'W_top1': W_top1, 'b_top1': b_top1, 'W_top2': W_top2, 'b_top2': b_top2, 'W_top3': W_top3}

def reference(r_bottom_mlp_out, ids, tbl_0, tbl_1, tbl_2, tbl_3, tbl_4, tbl_5, tbl_6, tbl_7, tbl_8, tbl_9, tbl_10, tbl_11, tbl_12, tbl_13, tbl_14, tbl_15, tbl_16, tbl_17, tbl_18, tbl_19, tbl_20, tbl_21, tbl_22, tbl_23, tbl_24, tbl_25, tbl_26, W_top1, b_top1, W_top2, b_top2, W_top3):
    import jax
    import jax.numpy as jnp

    def _L0_rec_ref(features, bottom_mlp_out):
        import jax, jax.numpy as jnp
        import numpy as np
        NUM_FEATURES = 27

        def _tril_indices(F):
            idx = []
            for i in range(F):
                for j in range(i):
                    idx.append(i * F + j)
            return np.asarray(idx, dtype=np.int32)
        TRIL_IDX = _tril_indices(NUM_FEATURES)
        B = features.shape[0]
        F = features.shape[1]
        interactions = jnp.einsum('bfd,bgd->bfg', features, features)
        interactions = interactions.reshape(B, F * F)
        x = interactions[:, TRIL_IDX]
        return jnp.concatenate([bottom_mlp_out, x], axis=1)
    e = jnp.stack([tbl_0[ids[:, 0]], tbl_1[ids[:, 1]], tbl_2[ids[:, 2]], tbl_3[ids[:, 3]], tbl_4[ids[:, 4]], tbl_5[ids[:, 5]], tbl_6[ids[:, 6]], tbl_7[ids[:, 7]], tbl_8[ids[:, 8]], tbl_9[ids[:, 9]], tbl_10[ids[:, 10]], tbl_11[ids[:, 11]], tbl_12[ids[:, 12]], tbl_13[ids[:, 13]], tbl_14[ids[:, 14]], tbl_15[ids[:, 15]], tbl_16[ids[:, 16]], tbl_17[ids[:, 17]], tbl_18[ids[:, 18]], tbl_19[ids[:, 19]], tbl_20[ids[:, 20]], tbl_21[ids[:, 21]], tbl_22[ids[:, 22]], tbl_23[ids[:, 23]], tbl_24[ids[:, 24]], tbl_25[ids[:, 25]], tbl_26[ids[:, 26]]], axis=1)
    z = _L0_rec_ref(e, r_bottom_mlp_out)
    z = z.reshape(z.shape[0], -1)
    h = jnp.concatenate([z, r_bottom_mlp_out], axis=1)
    h = jnp.maximum(h @ W_top1 + b_top1, 0.0)
    h = jnp.maximum(h @ W_top2 + b_top2, 0.0)
    y = h @ W_top3
    return y

_drawn_inputs = setup_inputs


def setup_inputs(seed=0):
    import zlib

    import numpy as np

    out = dict(_drawn_inputs(seed))
    spreads = {'b_top1': (0.0, 0.1), 'b_top2': (0.0, 0.1)}
    factors = {'tbl_0': 4.699,
     'tbl_1': 5.18,
     'tbl_2': 4.467,
     'tbl_3': 4.228,
     'tbl_4': 4.967,
     'tbl_5': 4.366,
     'tbl_6': 4.52,
     'tbl_7': 3.903,
     'tbl_8': 4.637,
     'tbl_9': 5.073,
     'tbl_10': 4.555,
     'tbl_11': 4.195,
     'tbl_12': 4.54,
     'tbl_13': 4.431,
     'tbl_14': 4.775,
     'tbl_15': 4.867,
     'tbl_16': 4.888,
     'tbl_17': 5.133,
     'tbl_18': 3.871,
     'tbl_19': 4.238,
     'tbl_20': 4.083,
     'tbl_21': 5.309,
     'tbl_22': 4.828,
     'tbl_23': 4.866,
     'tbl_24': 4.286,
     'tbl_25': 5.297,
     'tbl_26': 4.393}
    for name, (base, spread) in spreads.items():
        noise = np.random.default_rng([zlib.crc32(name.encode()), seed]).standard_normal(out[name].shape)
        drawn = base * np.exp(spread * noise) if base else spread * noise
        out[name] = jnp.asarray(drawn.astype(out[name].dtype))
    for name, factor in factors.items():
        out[name] = (out[name] * factor).astype(out[name].dtype)
    return out
```

```python
from contextlib import ExitStack

import concourse.bass as bass
from concourse import mybir

F32 = mybir.dt.float32
I32 = mybir.dt.int32
ALU = mybir.AluOpType
ACT = mybir.ActivationFunctionType

P = 128
QUAD = 32
NQ = P // QUAD


def build_dlrm(nc, bottom_in, ids_in, tables, W1_in, b1_in, W2_in, b2_in, W3_in, out):
    B, F = ids_in.shape
    D = bottom_in.shape[1]
    H1, H2 = W1_in.shape[1], W2_in.shape[1]
    TILES = B // P
    M1, M2 = H1 // P, H2 // P
    NPAIR = F * (F - 1) // 2
    COLS = F - 1
    JB = -(-COLS // NQ)
    FG = 4
    GROUPS = [range(g, min(g + FG, F)) for g in range(0, F, FG)]
    NG = len(GROUPS)
    DVE_GROUPS = [g for g in range(NG) if g % 2 == 0]
    ACT_GROUPS = [g for g in range(NG) if g % 2 == 1]
    ND, NA = len(DVE_GROUPS), len(ACT_GROUPS)
    CHUNK = 8
    CHUNKS = QUAD // CHUNK
    assert D == P and B % P == 0 and F <= QUAD and W1_in.shape[0] == 2 * D + NPAIR and CHUNKS % 2 == 0

    with ExitStack() as ctx:
        def sb(name, shape, dt=F32):
            return ctx.enter_context(nc.sbuf_tensor(name, shape, dt))

        def psum(name, shape):
            return ctx.enter_context(nc.psum_tensor(name, shape, F32))

        def sem(name):
            return ctx.enter_context(nc.semaphore(name))

        ids = sb("ids", [P, (TILES + 1) * F], I32)
        ids_now = sb("ids_now", [P, F], I32)
        rows = sb("rows", [P, F, D])
        embed = sb("embed", [P, QUAD, NQ, QUAD])
        pairs = sb("pairs", [P, JB, P])
        bottom = sb("bottom", [P, TILES, D])
        bottomT = sb("bottomT", [P, TILES * P])
        ident = sb("ident", [P, P])
        w_pairs = sb("w_pairs", [P, JB, H1])
        w_bot = sb("w_bot", [P, 2, H1])
        w_bottom = sb("w_bottom", [P, H1])
        w2 = sb("w2", [P, M1, H2])
        vec_rows = sb("vec_rows", [M1 + 2 * M2, P])
        vecs = sb("vecs", [P, M1 + 2 * M2])
        b1, b2, w3 = vecs[:, 0:M1], vecs[:, M1:M1 + M2], vecs[:, M1 + M2:]
        h1 = sb("h1", [P, M1, P])
        h2 = sb("h2", [P, M2, P])
        y = sb("y", [1, B])

        turned = [psum(f"turned{k}", [P, FG, P]) for k in range(2)]
        gram = [psum(f"gram{k}", [P, CHUNK, P]) for k in range(2)]
        h1_ps = [psum(f"h1_ps{k}", [P, M1 // 2, 2 * P]) for k in range(2)]
        h2_ps = [gram[k][:, 0:M2 // 2, :] for k in range(2)]
        y_ps = gram[1][0:1, CHUNK - 1, :]

        bottom_ps = gram[0][:, 0:TILES, :]
        vecs_ps = gram[0][:, TILES, 0:M1 + 2 * M2]

        ids_loaded = sem("ids_loaded")
        bottom_loaded = sem("bottom_loaded")
        w_bot_loaded = sem("w_bot_loaded")
        w_pairs_loaded = sem("w_pairs_loaded")
        w2_loaded = sem("w2_loaded")
        vecs_loaded = sem("vecs_loaded")
        vecs_turned = sem("vecs_turned")
        vecs_ready = sem("vecs_ready")
        gathered = [sem(f"gathered{f}") for f in range(F)]
        ids_padded = sem("ids_padded")
        ids_staged = sem("ids_staged")
        group_started = sem("group_started")
        zeros_set = sem("zeros_set")
        w_zeroed = sem("w_zeroed")
        ident_zeroed = sem("ident_zeroed")
        ident_ready = sem("ident_ready")
        w_bottom_ready = sem("w_bottom_ready")
        bottom_turned = sem("bottom_turned")
        bottomT_ready = sem("bottomT_ready")
        group_turned = sem("group_turned")
        embed_by_dve = sem("embed_by_dve")
        embed_by_act = sem("embed_by_act")
        gram_ready = sem("gram_ready")
        pairs_by_dve = sem("pairs_by_dve")
        pairs_by_act = sem("pairs_by_act")
        h1_summed = sem("h1_summed")
        h1_by_dve = sem("h1_by_dve")
        h1_by_act = sem("h1_by_act")
        h2_summed = sem("h2_summed")
        h2_by_dve = sem("h2_by_dve")
        h2_by_act = sem("h2_by_act")
        y_summed = sem("y_summed")
        y_ready = sem("y_ready")
        y_stored = sem("y_stored")

        block = ctx.enter_context(nc.Block())

        def h1_half(m):
            return h1_ps[m // (M1 // 2)][:, m % (M1 // 2), 0:P]

        def h2_half(m):
            return h2_ps[m // (M2 // 2)][:, m % (M2 // 2), :]

        def copy_group(copy, g):
            n = len(GROUPS[g])
            return copy(embed[:, :, :, g * FG:g * FG + n].rearrange("d g q f -> d q g f"),
                        turned[g % 2][:, 0:n, :].rearrange("d f (q g) -> d q g f", q=NQ))

        def copy_pairs(copy, c, q):
            for lane in range(NQ):
                n = len(range(lane, COLS, NQ))
                first = q * COLS + lane
                src = gram[c % 2][q * QUAD:(q + 1) * QUAD, :, first:first + NQ * (n - 1) + 1:NQ]
                s0 = q * QUAD + c * CHUNK
                last = copy(pairs[lane * QUAD:(lane + 1) * QUAD, 0:n, s0:s0 + CHUNK],
                            src.rearrange("i g j -> i j g"))
            return last

        @block.sync
        def _(sp):
            sp.dma_start(ids[:, 0:TILES * F], ids_in.rearrange("(p t) f -> p (t f)", t=TILES)).then_inc(ids_loaded, 16)
            sp.dma_start(bottom[:, :, :], bottom_in.rearrange("(p t) d -> p t d", t=TILES)).then_inc(bottom_loaded, 16)
            sp.dma_start(vec_rows[0:M1, :], b1_in.rearrange("(m p) -> m p", p=P)).then_inc(vecs_loaded, 16)
            sp.dma_start(vec_rows[M1:M1 + M2, :], b2_in.rearrange("(m p) -> m p", p=P)).then_inc(vecs_loaded, 16)
            sp.dma_start(vec_rows[M1 + M2:, :], W3_in.rearrange("(m p) o -> m (p o)", p=P)).then_inc(vecs_loaded, 16)
            sp.dma_start(w_bot[:, 0, :], W1_in[0:D, :]).then_inc(w_bot_loaded, 16)
            sp.dma_start(w_bot[:, 1, :], W1_in[D + NPAIR:, :]).then_inc(w_bot_loaded, 16)
            sp.wait_ge(w_zeroed, 1)
            for j in range(1, F):
                lane, jb = (j - 1) % NQ, (j - 1) // NQ
                r0 = D + j * (j - 1) // 2
                sp.dma_start(w_pairs[lane * QUAD:lane * QUAD + j, jb, :],
                             W1_in[r0:r0 + j, :]).then_inc(w_pairs_loaded, 16)
            sp.dma_start(w2[:, :, :], W2_in.rearrange("(m p) n -> p m n", p=P)).then_inc(w2_loaded, 16)
            sp.wait_ge(y_ready, TILES)
            sp.dma_start(out.rearrange("b o -> o b"), y[:, :]).then_inc(y_stored, 16)
            sp.wait_ge(y_stored, 16)

        @block.gpsimd
        def _(pool):
            pool.memset(ident[:, :], 0.0).then_inc(ident_zeroed, 1)
            pool.wait_ge(ident_zeroed, 1)
            pool.affine_select(out=ident[:, :], in_=ident[:, :], compare_op=ALU.not_equal, fill=1.0,
                               base=0, pattern=[[-1, P]], channel_multiplier=1).then_inc(ident_ready, 1)
            with pool.Fori(0, TILES) as t:
                for f in range(F):
                    if f % FG == 0:
                        pool.wait_ge(ids_staged, t * NG + f // FG + 1)
                        pool.sem_inc(group_started, 1)
                    pool.indirect_dma_start(
                        out=rows[:, f, :], out_offset=None, in_=tables[f],
                        in_offset=bass.IndirectOffsetOnAxis(ap=ids_now[:, f:f + 1], axis=0),
                    ).then_inc(gathered[f], 16)

        @block.tensor
        def _(pe):
            pe.wait_ge(ident_ready, 1)
            pe.wait_ge(bottom_loaded, 16)
            for t in range(TILES):
                last = pe.transpose(bottom_ps[:, t, :], bottom[:, t, :], ident[:, :])
            last.then_inc(bottom_turned, 1)
            pe.wait_ge(vecs_loaded, 48)
            pe.transpose(vecs_ps, vec_rows[:, :], ident[0:M1 + 2 * M2, 0:M1 + 2 * M2]).then_inc(vecs_turned, 1)
            pe.wait_ge(zeros_set, 1)
            pe.wait_ge(bottomT_ready, 1)
            pe.wait_ge(vecs_ready, 1)

            def transposes(t, first):
                for g in range(NG):
                    if g % 2 == 0 and not (first and g == 0):
                        pe.wait_ge(embed_by_dve, t * ND + g // 2)
                    if g % 2 == 1 and not (first and g == 1):
                        pe.wait_ge(embed_by_act, t * NA + g // 2)
                    for k, f in enumerate(GROUPS[g]):
                        pe.wait_ge(gathered[f], (t + 1) * 16)
                        last = pe.transpose(turned[g % 2][:, k, :], rows[:, f, :], ident[:, :])
                    last.then_inc(group_turned, 1)

            def grams(t, first):
                pe.wait_ge(embed_by_dve, (t + 1) * ND)
                pe.wait_ge(embed_by_act, (t + 1) * NA)
                for c in range(CHUNKS):
                    if not (first and c < 2):
                        pe.wait_ge(pairs_by_dve, t * CHUNKS + c - 1)
                        pe.wait_ge(pairs_by_act, t * CHUNKS + c - 1)
                    for g in range(CHUNK):
                        four = embed[:, c * CHUNK + g, :, :]
                        last = pe.matmul(gram[c % 2][:, g, 0:NQ * COLS],
                                         four, four[:, :, 1:F], start=True, stop=True)
                    last.then_inc(gram_ready, 1)

            def mlp(t):
                pe.wait_ge(pairs_by_dve, (t + 1) * CHUNKS)
                pe.wait_ge(pairs_by_act, (t + 1) * CHUNKS)
                for m in range(M1):
                    cols = slice(m * P, (m + 1) * P)
                    pe.matmul(h1_half(m), w_bottom[:, cols], bottomT[:, bass.ds(t * P, P)],
                              start=True, stop=False)
                    for jb in range(JB):
                        last = pe.matmul(h1_half(m), w_pairs[:, jb, cols], pairs[:, jb, :],
                                         start=False, stop=(jb == JB - 1))
                last.then_inc(h1_summed, 1)
                pe.wait_ge(h1_by_dve, t + 1)
                pe.wait_ge(h1_by_act, t + 1)
                for m in range(M2):
                    for k in range(M1):
                        last = pe.matmul(h2_half(m), w2[:, k, m * P:(m + 1) * P], h1[:, k, :],
                                         start=(k == 0), stop=(k == M1 - 1))
                last.then_inc(h2_summed, 1)
                pe.wait_ge(h2_by_dve, t + 1)
                pe.wait_ge(h2_by_act, t + 1)
                for k in range(M2):
                    last = pe.matmul(y_ps, w3[:, k:k + 1], h2[:, k, :],
                                     start=(k == 0), stop=(k == M2 - 1))
                last.then_inc(y_summed, 1)

            transposes(0, True)
            grams(0, True)
            pe.wait_ge(w_bottom_ready, 1)
            pe.wait_ge(w_pairs_loaded, 16 * COLS)
            pe.wait_ge(w2_loaded, 16)
            mlp(0)
            with pe.Fori(1, TILES) as t:
                transposes(t, False)
                pe.wait_ge(y_ready, t)
                grams(t, False)
                mlp(t)

        @block.vector
        def _(dve):
            def stage_ids(t, g):
                n = len(GROUPS[g])
                dve.tensor_copy(ids_now[:, g * FG:g * FG + n],
                                ids[:, bass.ds(t * F + g * FG, n)]).then_inc(ids_staged, 1)

            dve.memset(ids[:, TILES * F:], 0).then_inc(ids_padded, 1)
            dve.wait_ge(ids_padded, 1)
            dve.wait_ge(ids_loaded, 16)
            for g in range(NG):
                stage_ids(0, g)
            dve.memset(w_pairs[:, :, :], 0.0).then_inc(w_zeroed, 1)
            dve.memset(embed[:, :, :, F:QUAD], 0.0)
            dve.memset(pairs[:, JB - 1, :], 0.0).then_inc(zeros_set, 1)
            dve.wait_ge(zeros_set, 1)
            dve.wait_ge(bottom_turned, 1)
            dve.tensor_copy(bottomT[:, :], bottom_ps.rearrange("p t s -> p (t s)")).then_inc(bottomT_ready, 1)
            dve.wait_ge(w_bot_loaded, 32)
            dve.tensor_tensor(w_bottom[:, :], w_bot[:, 0, :], w_bot[:, 1, :], ALU.add).then_inc(w_bottom_ready, 1)
            dve.wait_ge(vecs_turned, 1)
            dve.tensor_copy(vecs[:, :], vecs_ps).then_inc(vecs_ready, 1)
            dve.wait_ge(vecs_ready, 1)
            with dve.Fori(0, TILES) as t:
                for g in range(NG):
                    dve.wait_ge(group_turned, t * NG + g + 1)
                    stage_ids(t + 1, g)
                    if g in DVE_GROUPS:
                        copy_group(dve.tensor_copy, g).then_inc(embed_by_dve, 1)
                for c in range(CHUNKS):
                    dve.wait_ge(gram_ready, t * CHUNKS + c + 1)
                    copy_pairs(dve.tensor_copy, c, 0)
                    copy_pairs(dve.tensor_copy, c, 1).then_inc(pairs_by_dve, 1)
                dve.wait_ge(h1_summed, t + 1)
                for m in range(M1 // 2):
                    last = dve.tensor_scalar(h1[:, m, :], h1_half(m), b1[:, m:m + 1], 0.0, ALU.add, ALU.max)
                last.then_inc(h1_by_dve, 1)
                dve.wait_ge(h2_summed, t + 1)
                for m in range(M2 // 2):
                    last = dve.tensor_scalar(h2[:, m, :], h2_half(m), b2[:, m:m + 1], 0.0, ALU.add, ALU.max)
                last.then_inc(h2_by_dve, 1)

        @block.scalar
        def _(act):
            act.wait_ge(zeros_set, 1)
            act.wait_ge(vecs_ready, 1)
            with act.Fori(0, TILES) as t:
                for g in ACT_GROUPS:
                    act.wait_ge(group_turned, t * NG + g + 1)
                    copy_group(act.copy, g).then_inc(embed_by_act, 1)
                for c in range(CHUNKS):
                    act.wait_ge(gram_ready, t * CHUNKS + c + 1)
                    copy_pairs(act.copy, c, 2)
                    copy_pairs(act.copy, c, 3).then_inc(pairs_by_act, 1)
                act.wait_ge(h1_summed, t + 1)
                for m in range(M1 // 2, M1):
                    last = act.activation(h1[:, m, :], h1_half(m), ACT.Relu, bias=b1[:, m:m + 1])
                last.then_inc(h1_by_act, 1)
                act.wait_ge(h2_summed, t + 1)
                for m in range(M2 // 2, M2):
                    last = act.activation(h2[:, m, :], h2_half(m), ACT.Relu, bias=b2[:, m:m + 1])
                last.then_inc(h2_by_act, 1)
                act.wait_ge(y_summed, t + 1)
                act.copy(y[0:1, bass.ds(t, P, TILES)], y_ps).then_inc(y_ready, 1)


def kernel(**inputs):
    import numpy as np
    import concourse.bacc as bacc
    from concourse.bass_utils import run_bass_kernel_spmd as run

    F = inputs["ids"].shape[1]
    names = (["r_bottom_mlp_out", "ids"] + [f"tbl_{f}" for f in range(F)]
             + ["W_top1", "b_top1", "W_top2", "b_top2", "W_top3"])
    nc = bacc.Bacc("TRN2", target_bir_lowering=False, num_devices=1)
    arrays, aps = {}, {}
    for name in names:
        a = np.ascontiguousarray(inputs[name])
        arrays[f"in_{name}"] = a
        aps[name] = nc.dram_tensor(f"in_{name}", a.shape, mybir.dt.from_np(a.dtype), kind="ExternalInput").ap()
    out = nc.dram_tensor("out_y", (inputs["ids"].shape[0], 1), F32, kind="ExternalOutput").ap()
    build_dlrm(nc, aps["r_bottom_mlp_out"], aps["ids"], [aps[f"tbl_{f}"] for f in range(F)],
               aps["W_top1"], aps["b_top1"], aps["W_top2"], aps["b_top2"], aps["W_top3"], out)
    return run(nc, [arrays], core_ids=[0]).results[0]["out_y"]
```

```python
from contextlib import ExitStack

import concourse.bass as bass
from concourse import mybir

F32 = mybir.dt.float32
F32R = mybir.dt.float32r
I32 = mybir.dt.int32
ALU = mybir.AluOpType
ACT = mybir.ActivationFunctionType

P = 128
QUAD = 32
NQ = P // QUAD
FG = 4
HOT_MOST = 5


def runs(features):
    found = []
    for f in features:
        if found and found[-1][0] + found[-1][1] == f:
            found[-1][1] += 1
        else:
            found.append([f, 1])
    return [tuple(r) for r in found]


def build_dlrm(nc, bottom_in, ids_in, tables, W1_in, b1_in, W2_in, b2_in, W3_in, out):
    B, F = ids_in.shape
    D = bottom_in.shape[1]
    H1, H2 = W1_in.shape[1], W2_in.shape[1]
    TILES = B // P
    LAST = TILES - 1
    M1, M2 = H1 // P, H2 // P
    NPAIR = F * (F - 1) // 2
    COLS = F - 1
    JB = -(-COLS // NQ)
    NVEC = M1 + 2 * M2

    SMALL = [f for f in range(F) if tables[f].shape[0] <= 8 * P]
    HOT = SMALL[-HOT_MOST:]
    NH = len(HOT)
    VH = tables[HOT[0]].shape[0]
    KT = -(-VH // P)
    VP = VH // KT
    assert VP * KT == VH and all(tables[f].shape[0] == VH for f in HOT)

    GROUPS = [list(range(f, min(f + FG, a + n))) for a, n in runs([f for f in range(F) if f not in HOT])
              for f in range(a, a + n, FG)]
    NG = len(GROUPS)
    AFTER_GRAM, IN_LAYER1, AFTER_LAYER1, AFTER_LAYER2, AFTER_LAYER3 = (
        range(0, 1), range(1, 2), range(2, 4), range(4, 5), range(5, NG))

    def dve_has(g):
        return g % 2 == 0

    def first_tile_groups(h):
        return range(2 * h, min(2 * h + 2, NG)) if h < NH - 1 else range(min(2 * h, NG), NG)

    ND = sum(dve_has(g) for g in range(NG))
    NA = NG - ND
    CHUNK = 8
    CHUNKS = QUAD // CHUNK
    GW = P
    assert D == P and B % P == 0 and F <= QUAD and W1_in.shape[0] == 2 * D + NPAIR
    assert NQ * COLS <= GW

    with ExitStack() as ctx:
        def sb(name, shape, dt=F32):
            return ctx.enter_context(nc.sbuf_tensor(name, shape, dt))

        def psum(name, shape):
            return ctx.enter_context(nc.psum_tensor(name, shape, F32))

        def sem(name):
            return ctx.enter_context(nc.semaphore(name))

        ids = sb("ids", [P, (TILES + 1) * F], I32)
        ids_now = sb("ids_now", [P, F], I32)
        ids_float = sb("ids_float", [P, TILES, F])
        idsT = sb("idsT", [F, TILES * P], F32R)
        pick = sb("pick", [F, NH, P], F32R)
        hot_ids = sb("hot_ids", [P, NH, TILES * P])
        row_ints = sb("row_ints", [P, KT], I32)
        row_number = sb("row_number", [P, KT])
        table_raw = sb("table_raw", [P, 2, KT * D])
        table_hi = sb("table_hi", [P, 2, KT * D], F32R)
        table_lo = sb("table_lo", [P, 2, KT * D], F32R)
        onehot = sb("onehot", [P, 2, KT, TILES * P], F32R)
        found = sb("found", [P, NH, TILES * P])
        rows = sb("rows", [P, F - NH, D])
        embed = sb("embed", [P, QUAD, NQ, QUAD])
        pairs = sb("pairs", [P, JB, P])
        bottom = sb("bottom", [P, TILES, D])
        bottomT = sb("bottomT", [P, TILES * P])
        ident = sb("ident", [P, P])
        w_pairs = sb("w_pairs", [P, JB, H1])
        w_bot = sb("w_bot", [P, 2, H1])
        w_bottom = sb("w_bottom", [P, H1])
        w2 = sb("w2", [P, M1, H2])
        vec_rows = sb("vec_rows", [NVEC, P])
        vecs = sb("vecs", [P, NVEC])
        b1, b2, w3 = vecs[:, 0:M1], vecs[:, M1:M1 + M2], vecs[:, M1 + M2:]
        h1 = sb("h1", [P, M1, P])
        h2 = sb("h2", [P, M2, P])
        y = sb("y", [1, B])

        turned = [psum(f"turned{k}", [P, FG, P]) for k in range(2)]
        gram = [psum(f"gram{k}", [P, CHUNK * GW]) for k in range(2)]
        h1_ps = [psum(f"h1_ps{k}", [P, 4 * P]) for k in range(2)]
        y_ps = gram[1][0:1, 4 * P:5 * P]
        bottom_ps, idsT_ps, vecs_ps = h1_ps[0], h1_ps[1], turned[0][:, 0, 0:NVEC]
        found_ps = [gram[k][:, 0:TILES * P] for k in range(2)]
        hot_ids_ps = [gram[k][:, 4 * P:4 * P + TILES * P] for k in range(2)]

        ids_loaded = sem("ids_loaded")
        bottom_loaded = sem("bottom_loaded")
        w_bot_loaded = sem("w_bot_loaded")
        w_pairs_loaded = sem("w_pairs_loaded")
        w2_loaded = sem("w2_loaded")
        vecs_loaded = sem("vecs_loaded")
        table_loaded = [sem(f"table_loaded{h}") for h in range(NH)]
        gathered = [sem(f"gathered{f}") for f in range(F)]
        ids_padded = sem("ids_padded")
        ids_staged = sem("ids_staged")
        group_started = sem("group_started")
        w_zeroed = sem("w_zeroed")
        ident_zeroed = sem("ident_zeroed")
        ident_ready = sem("ident_ready")
        rows_counted = sem("rows_counted")
        zeros_set = sem("zeros_set")
        ids_floated = sem("ids_floated")
        row_number_set = sem("row_number_set")
        idsT_turned = sem("idsT_turned")
        idsT_ready = sem("idsT_ready")
        pick_ready = sem("pick_ready")
        hot_ids_spread = sem("hot_ids_spread")
        hot_ids_ready = sem("hot_ids_ready")
        table_hi_ready = sem("table_hi_ready")
        table_split = sem("table_split")
        onehot_ready = sem("onehot_ready")
        hot_summed = sem("hot_summed")
        found_ready = sem("found_ready")
        w_bottom_ready = sem("w_bottom_ready")
        bottom_turned = sem("bottom_turned")
        bottomT_ready = sem("bottomT_ready")
        vecs_turned = sem("vecs_turned")
        vecs_ready = sem("vecs_ready")
        group_turned = sem("group_turned")
        embed_by_dve = sem("embed_by_dve")
        embed_by_act = sem("embed_by_act")
        hot_by_act = sem("hot_by_act")
        gram_ready = sem("gram_ready")
        pairs_by_dve = sem("pairs_by_dve")
        pairs_by_act = sem("pairs_by_act")
        h1_summed = sem("h1_summed")
        h1_by_dve = sem("h1_by_dve")
        h1_by_act = sem("h1_by_act")
        h2_summed = sem("h2_summed")
        h2_by_dve = sem("h2_by_dve")
        h2_by_act = sem("h2_by_act")
        y_summed = sem("y_summed")
        gram_free = sem("gram_free")
        y_ready = sem("y_ready")
        y_stored = sem("y_stored")

        block = ctx.enter_context(nc.Block())

        cold_slot = {f: k for k, f in enumerate(f for g in GROUPS for f in g)}

        def h1_half(m):
            k = m // (M1 // 2)
            return h1_ps[k][:, (m - k * M1 // 2) * P:(m - k * M1 // 2 + 1) * P]

        def h2_half(m):
            return gram[m // (M2 // 2)][:, (m % (M2 // 2)) * P:(m % (M2 // 2) + 1) * P]

        def copy_group(copy, g):
            f, n = GROUPS[g][0], len(GROUPS[g])
            return copy(embed[:, :, :, f:f + n].rearrange("d g q f -> d q g f"),
                        turned[g % 2][:, 0:n, :].rearrange("d f (q g) -> d q g f", q=NQ))

        def copy_pairs(copy, c, quarters):
            for q in quarters:
                own = gram[c % 2][q * QUAD:(q + 1) * QUAD, :].rearrange("i (g c) -> i c g", c=GW)
                s0 = q * QUAD + c * CHUNK
                for lane in range(NQ):
                    n = len(range(lane, COLS, NQ))
                    first = q * COLS + lane
                    last = copy(pairs[lane * QUAD:(lane + 1) * QUAD, 0:n, s0:s0 + CHUNK],
                                own[:, first:first + NQ * (n - 1) + 1:NQ, :])
            return last

        @block.sync
        def _(sp):
            sp.dma_start(ids[:, 0:TILES * F], ids_in.rearrange("(p t) f -> p (t f)", t=TILES)).then_inc(ids_loaded, 16)

            def load_table(h):
                src = tables[HOT[h]].rearrange("(p k) d -> p (k d)", k=KT)
                for a, b in ((0, VP // 16 * 16), (VP // 16 * 16, VP)):
                    sp.dma_start(table_raw[a:b, h % 2, :], src[a:b, :]).then_inc(table_loaded[h], 16)

            load_table(0)
            load_table(1)
            sp.dma_start(bottom[:, :, :], bottom_in.rearrange("(p t) d -> p t d", t=TILES)).then_inc(bottom_loaded, 16)
            sp.dma_start(vec_rows[0:M1, :], b1_in.rearrange("(m p) -> m p", p=P)).then_inc(vecs_loaded, 16)
            sp.dma_start(vec_rows[M1:M1 + M2, :], b2_in.rearrange("(m p) -> m p", p=P)).then_inc(vecs_loaded, 16)
            sp.dma_start(vec_rows[M1 + M2:, :], W3_in.rearrange("(m p) o -> m (p o)", p=P)).then_inc(vecs_loaded, 16)
            sp.wait_ge(w_zeroed, 2)
            for h in range(2, NH):
                sp.wait_ge(table_split, h - 1)
                load_table(h)
                for j in range(h - 1, F, NH - 2):
                    lane, jb = (j - 1) % NQ, (j - 1) // NQ
                    r0 = D + j * (j - 1) // 2
                    sp.dma_start(w_pairs[lane * QUAD:lane * QUAD + j, jb, :],
                                 W1_in[r0:r0 + j, :]).then_inc(w_pairs_loaded, 16)
            sp.dma_start(w_bot[:, 0, :], W1_in[0:D, :]).then_inc(w_bot_loaded, 16)
            sp.dma_start(w_bot[:, 1, :], W1_in[D + NPAIR:, :]).then_inc(w_bot_loaded, 16)
            sp.dma_start(w2[:, :, :], W2_in.rearrange("(m p) n -> p m n", p=P)).then_inc(w2_loaded, 16)
            sp.wait_ge(y_ready, TILES)
            sp.dma_start(out.rearrange("b o -> o b"), y[:, :]).then_inc(y_stored, 16)
            sp.wait_ge(y_stored, 16)

        @block.gpsimd
        def _(pool):
            pool.memset(ident[:, :], 0.0).then_inc(ident_zeroed, 1)
            pool.wait_ge(ident_zeroed, 1)
            pool.affine_select(out=ident[:, :], in_=ident[:, :], compare_op=ALU.not_equal, fill=1.0,
                               base=0, pattern=[[-1, P]], channel_multiplier=1).then_inc(ident_ready, 1)
            pool.iota(row_ints[:, :], [[1, KT]], 0, KT).then_inc(rows_counted, 1)
            pool.memset(w_pairs[:, JB - JB // 3:, :], 0.0).then_inc(w_zeroed, 1)
            with pool.Fori(0, TILES) as t:
                for n, group in enumerate(GROUPS):
                    pool.wait_ge(ids_staged, t * NG + n + 1)
                    pool.sem_inc(group_started, 1)
                    for f in group:
                        pool.indirect_dma_start(
                            out=rows[:, cold_slot[f], :], out_offset=None, in_=tables[f],
                            in_offset=bass.IndirectOffsetOnAxis(ap=ids_now[:, f:f + 1], axis=0),
                        ).then_inc(gathered[f], 16)

        @block.tensor
        def _(pe):
            pe.wait_ge(ident_ready, 1)
            pe.wait_ge(ids_floated, 1)
            for t in range(TILES):
                last = pe.transpose(idsT_ps[0:F, t * P:(t + 1) * P], ids_float[:, t, :], ident[:, :])
            last.then_inc(idsT_turned, 1)
            pe.wait_ge(idsT_ready, 1)
            pe.wait_ge(pick_ready, 1)

            def spread_ids(h):
                if h >= 2:
                    pe.wait_ge(hot_ids_ready, h - 1)
                pe.matmul(hot_ids_ps[h % 2], pick[:, h, :], idsT[:, :], start=True, stop=True).then_inc(hot_ids_spread, 1)

            spread_ids(0)
            spread_ids(1)
            pe.wait_ge(bottom_loaded, 16)
            for t in range(TILES):
                last = pe.transpose(bottom_ps[:, t * P:(t + 1) * P], bottom[:, t, :], ident[:, :])
            last.then_inc(bottom_turned, 1)
            pe.wait_ge(vecs_loaded, 48)
            pe.transpose(vecs_ps, vec_rows[:, :], ident[0:NVEC, 0:NVEC]).then_inc(vecs_turned, 1)
            pe.wait_ge(vecs_ready, 1)

            def turn(t, groups, first=False):
                for g in groups or ():
                    if dve_has(g) and not (first and g == 0):
                        pe.wait_ge(embed_by_dve, t * ND + g // 2)
                    if not dve_has(g) and not (first and g == 1):
                        pe.wait_ge(embed_by_act, t * NA + g // 2)
                    for k, f in enumerate(GROUPS[g]):
                        pe.wait_ge(gathered[f], (t + 1) * 16)
                        last = pe.transpose(turned[g % 2][:, k, :], rows[:, cold_slot[f], :], ident[:, :])
                    last.then_inc(group_turned, 1)

            def look_up(h):
                pe.wait_ge(table_split, h + 1)
                if h >= 2:
                    pe.wait_ge(found_ready, h - 1)
                for kt in range(KT):
                    pe.wait_ge(onehot_ready, h * KT + kt + 1)
                    for part in (table_hi, table_lo):
                        last = pe.matmul(found_ps[h % 2], part[0:VP, h % 2, kt * D:(kt + 1) * D],
                                         onehot[0:VP, h % 2, kt, :], start=(kt == 0 and part is table_hi),
                                         stop=(kt == KT - 1 and part is table_lo))
                last.then_inc(hot_summed, 1)

            def grams(t):
                pe.wait_ge(hot_by_act, t + 1)
                pe.wait_ge(embed_by_dve, (t + 1) * ND)
                pe.wait_ge(embed_by_act, (t + 1) * NA)
                pe.wait_ge(gram_free, t + 1)
                for c in range(CHUNKS):
                    if c >= 2:
                        pe.wait_ge(pairs_by_dve, t * CHUNKS + c - 1)
                        pe.wait_ge(pairs_by_act, t * CHUNKS + c - 1)
                    for g in range(CHUNK):
                        four = embed[:, c * CHUNK + g, :, :]
                        last = pe.matmul(gram[c % 2][:, g * GW:g * GW + NQ * COLS],
                                         four, four[:, :, 1:F], start=True, stop=True)
                    last.then_inc(gram_ready, 1)

            def layer1(t, ms):
                for m in ms:
                    cols = slice(m * P, (m + 1) * P)
                    pe.matmul(h1_half(m), w_bottom[:, cols], bottomT[:, bass.ds(t * P, P)],
                              start=True, stop=False)
                    for jb in range(JB):
                        last = pe.matmul(h1_half(m), w_pairs[:, jb, cols], pairs[:, jb, :],
                                         start=False, stop=(jb == JB - 1))
                return last

            def layer2(t):
                pe.wait_ge(h1_by_dve, t + 1)
                pe.wait_ge(h1_by_act, t + 1)
                for m in range(M2):
                    for k in range(M1):
                        last = pe.matmul(h2_half(m), w2[:, k, m * P:(m + 1) * P], h1[:, k, :],
                                         start=(k == 0), stop=(k == M1 - 1))
                last.then_inc(h2_summed, 1)

            def layer3(t):
                pe.wait_ge(h2_by_dve, t + 1)
                pe.wait_ge(h2_by_act, t + 1)
                for k in range(M2):
                    last = pe.matmul(y_ps, w3[:, k:k + 1], h2[:, k, :], start=(k == 0), stop=(k == M2 - 1))
                last.then_inc(y_summed, 1)

            def tile(t, turns):
                grams(t)
                turn(t + 1, turns and AFTER_GRAM)
                pe.wait_ge(pairs_by_dve, (t + 1) * CHUNKS)
                pe.wait_ge(pairs_by_act, (t + 1) * CHUNKS)
                layer1(t, range(M1 // 2))
                turn(t + 1, turns and IN_LAYER1)
                layer1(t, range(M1 // 2, M1)).then_inc(h1_summed, 1)
                turn(t + 1, turns and AFTER_LAYER1)
                layer2(t)
                turn(t + 1, turns and AFTER_LAYER2)
                layer3(t)
                turn(t + 1, turns and AFTER_LAYER3)

            pe.wait_ge(bottomT_ready, 1)
            pe.wait_ge(zeros_set, 2)
            for h in range(NH):
                if h + 2 < NH:
                    spread_ids(h + 2)
                look_up(h)
                turn(0, first_tile_groups(h), True)
            pe.wait_ge(w_bottom_ready, 1)
            pe.wait_ge(w_pairs_loaded, 16 * COLS)
            pe.wait_ge(w2_loaded, 16)
            with pe.Fori(0, LAST) as t:
                tile(t, True)
            tile(LAST, False)

        @block.vector
        def _(dve):
            def stage_ids(t, n):
                f, count = GROUPS[n][0], len(GROUPS[n])
                dve.tensor_copy(ids_now[:, f:f + count], ids[:, bass.ds(t * F + f, count)]).then_inc(ids_staged, 1)

            def split_table(h):
                dve.wait_ge(table_hi_ready, h + 1)
                if h >= 2:
                    dve.wait_ge(hot_summed, h - 1)
                dve.tensor_tensor(table_lo[0:VP, h % 2, :], table_raw[0:VP, h % 2, :], table_hi[0:VP, h % 2, :],
                                  ALU.subtract).then_inc(table_split, 1)

            def make_onehot(h):
                dve.wait_ge(hot_ids_ready, h + 1)
                for kt in range(KT):
                    dve.tensor_scalar(onehot[0:VP, h % 2, kt, :], hot_ids[0:VP, h, :],
                                      row_number[0:VP, kt:kt + 1], None, ALU.is_equal).then_inc(onehot_ready, 1)

            def groups(t, which):
                for g in which or ():
                    dve.wait_ge(group_turned, t * NG + g + 1)
                    stage_ids(t + 1, g)
                    if dve_has(g):
                        copy_group(dve.tensor_copy, g).then_inc(embed_by_dve, 1)

            def relu1(t):
                dve.wait_ge(h1_summed, t + 1)
                for m in range(M1 // 2):
                    last = dve.tensor_scalar(h1[:, m, :], h1_half(m), b1[:, m:m + 1], 0.0, ALU.add, ALU.max)
                last.then_inc(h1_by_dve, 1)

            def relu2(t):
                dve.wait_ge(h2_summed, t + 1)
                for m in range(M2 // 2):
                    last = dve.tensor_scalar(h2[:, m, :], h2_half(m), b2[:, m:m + 1], 0.0, ALU.add, ALU.max)
                last.then_inc(h2_by_dve, 1)

            dve.memset(ids[:, TILES * F:], 0).then_inc(ids_padded, 1)
            dve.memset(w_pairs[:, 0:JB - JB // 3, :], 0.0).then_inc(w_zeroed, 1)
            dve.wait_ge(ids_padded, 1)
            dve.wait_ge(ids_loaded, 16)
            for n in range(NG):
                stage_ids(0, n)
            dve.tensor_copy(ids_float[:, :, :].rearrange("p t f -> p (t f)"), ids[:, 0:TILES * F]).then_inc(ids_floated, 1)
            dve.wait_ge(rows_counted, 1)
            dve.tensor_copy(row_number[:, :], row_ints[:, :]).then_inc(row_number_set, 1)
            dve.memset(embed[:, :, :, F:QUAD], 0.0).then_inc(zeros_set, 1)
            dve.memset(pairs[:, JB - 1, :], 0.0).then_inc(zeros_set, 1)
            dve.wait_ge(idsT_turned, 1)
            dve.tensor_copy(idsT[:, :], idsT_ps[0:F, :]).then_inc(idsT_ready, 1)
            dve.wait_ge(row_number_set, 1)
            for h in range(NH):
                split_table(h)
                make_onehot(h)
                if h == 0:
                    dve.wait_ge(zeros_set, 2)
                else:
                    groups(0, first_tile_groups(h - 1))
            groups(0, first_tile_groups(NH - 1))
            dve.wait_ge(w_bot_loaded, 32)
            dve.tensor_tensor(w_bottom[:, :], w_bot[:, 0, :], w_bot[:, 1, :], ALU.add).then_inc(w_bottom_ready, 1)
            dve.wait_ge(vecs_ready, 1)

            def tile(t, turns):
                for c in range(CHUNKS):
                    dve.wait_ge(gram_ready, t * CHUNKS + c + 1)
                    copy_pairs(dve.tensor_copy, c, range(NQ // 2)).then_inc(pairs_by_dve, 1)
                groups(t + 1, turns and AFTER_GRAM)
                groups(t + 1, turns and IN_LAYER1)
                relu1(t)
                groups(t + 1, turns and AFTER_LAYER1)
                relu2(t)
                groups(t + 1, turns and AFTER_LAYER2)
                groups(t + 1, turns and AFTER_LAYER3)

            with dve.Fori(0, LAST) as t:
                tile(t, True)
            tile(LAST, False)

        @block.scalar
        def _(act):
            def groups(t, which):
                for g in which or ():
                    if not dve_has(g):
                        act.wait_ge(group_turned, t * NG + g + 1)
                        copy_group(act.copy, g).then_inc(embed_by_act, 1)

            def copy_hot(t):
                for f, n in runs(HOT):
                    h = HOT.index(f)
                    last = act.copy(embed[:, :, :, f:f + n].rearrange("d g q f -> d f q g"),
                                    found[:, h:h + n, bass.ds(t * P, P)].rearrange("d f (q g) -> d f q g", q=NQ))
                last.then_inc(hot_by_act, 1)

            def relu1(t):
                act.wait_ge(h1_summed, t + 1)
                for m in range(M1 // 2, M1):
                    last = act.activation(h1[:, m, :], h1_half(m), ACT.Relu, bias=b1[:, m:m + 1])
                last.then_inc(h1_by_act, 1)

            def relu2(t):
                act.wait_ge(h2_summed, t + 1)
                for m in range(M2 // 2, M2):
                    last = act.activation(h2[:, m, :], h2_half(m), ACT.Relu, bias=b2[:, m:m + 1])
                last.then_inc(h2_by_act, 1)

            def take_y(t):
                act.wait_ge(y_summed, t + 1)
                act.copy(y[0:1, bass.ds(t, P, TILES)], y_ps).then_inc(y_ready, 1)
                act.wait_ge(y_ready, t + 1)
                act.sem_inc(gram_free, 1)

            act.wait_ge(ident_ready, 1)
            for h, f in enumerate(HOT):
                last = act.copy(pick[:, h, :], ident[0:F, f:f + 1].broadcast_to([F, P]))
            last.then_inc(pick_ready, 1)

            def take_ids(h):
                act.wait_ge(hot_ids_spread, h + 1)
                act.copy(hot_ids[:, h, :], hot_ids_ps[h % 2]).then_inc(hot_ids_ready, 1)

            def take_hi(h):
                act.wait_ge(table_loaded[h], 32)
                act.copy(table_hi[0:VP, h % 2, :], table_raw[0:VP, h % 2, :]).then_inc(table_hi_ready, 1)

            take_hi(0)
            take_ids(0)
            take_ids(1)
            take_hi(1)
            act.wait_ge(bottom_turned, 1)
            act.copy(bottomT[:, :], bottom_ps[:, :]).then_inc(bottomT_ready, 1)
            act.wait_ge(vecs_turned, 1)
            act.copy(vecs[:, :], vecs_ps).then_inc(vecs_ready, 1)
            act.wait_ge(vecs_ready, 1)
            act.wait_ge(zeros_set, 2)
            for h in range(NH):
                if h + 2 < NH:
                    take_ids(h + 2)
                act.wait_ge(hot_summed, h + 1)
                act.copy(found[:, h, :], found_ps[h % 2]).then_inc(found_ready, 1)
                if h + 2 < NH:
                    take_hi(h + 2)
                groups(0, first_tile_groups(h))
            act.wait_ge(found_ready, NH)
            act.sem_inc(gram_free, 1)

            def tile(t, turns):
                for c in range(CHUNKS):
                    act.wait_ge(gram_ready, t * CHUNKS + c + 1)
                    copy_pairs(act.copy, c, range(NQ // 2, NQ)).then_inc(pairs_by_act, 1)
                groups(t + 1, turns and AFTER_GRAM)
                if turns:
                    copy_hot(t + 1)
                groups(t + 1, turns and IN_LAYER1)
                relu1(t)
                groups(t + 1, turns and AFTER_LAYER1)
                relu2(t)
                groups(t + 1, turns and AFTER_LAYER2)
                take_y(t)
                groups(t + 1, turns and AFTER_LAYER3)

            copy_hot(0)
            with act.Fori(0, LAST) as t:
                tile(t, True)
            tile(LAST, False)


def kernel(**inputs):
    import numpy as np
    import concourse.bacc as bacc
    from concourse.bass_utils import run_bass_kernel_spmd as run

    F = inputs["ids"].shape[1]
    names = (["r_bottom_mlp_out", "ids"] + [f"tbl_{f}" for f in range(F)]
             + ["W_top1", "b_top1", "W_top2", "b_top2", "W_top3"])
    nc = bacc.Bacc("TRN2", target_bir_lowering=False, num_devices=1)
    arrays, aps = {}, {}
    for name in names:
        a = np.ascontiguousarray(inputs[name])
        arrays[f"in_{name}"] = a
        aps[name] = nc.dram_tensor(f"in_{name}", a.shape, mybir.dt.from_np(a.dtype), kind="ExternalInput").ap()
    out = nc.dram_tensor("out_y", (inputs["ids"].shape[0], 1), F32, kind="ExternalOutput").ap()
    build_dlrm(nc, aps["r_bottom_mlp_out"], aps["ids"], [aps[f"tbl_{f}"] for f in range(F)],
               aps["W_top1"], aps["b_top1"], aps["W_top2"], aps["b_top2"], aps["W_top3"], out)
    return run(nc, [arrays], core_ids=[0]).results[0]["out_y"]
```

```python
from contextlib import ExitStack
from itertools import islice

import concourse.bass as bass
from concourse import mybir

F32 = mybir.dt.float32
F32R = mybir.dt.float32r
I32 = mybir.dt.int32
ALU = mybir.AluOpType
ACT = mybir.ActivationFunctionType

P = 128
QUAD = 32
NQ = P // QUAD
FG = 4
HOT_MOST = 7


def runs(features):
    found = []
    for f in features:
        if found and found[-1][0] + found[-1][1] == f:
            found[-1][1] += 1
        else:
            found.append([f, 1])
    return [tuple(r) for r in found]


def build_dlrm(nc, bottom_in, ids_in, tables, W1_in, b1_in, W2_in, b2_in, W3_in, out):
    B, F = ids_in.shape
    D = bottom_in.shape[1]
    H1, H2 = W1_in.shape[1], W2_in.shape[1]
    TILES = B // P
    LAST = TILES - 1
    M1, M2 = H1 // P, H2 // P
    NPAIR = F * (F - 1) // 2
    JB = 5
    assert F == 5 * JB + 2
    Z, X, Y, U = range(0, JB), range(JB, 4 * JB), range(4 * JB, 5 * JB), range(5 * JB, F)
    ROWS = [*X, *U, *Z, *Y, *U]
    SLOTS = [[r for r, g in enumerate(ROWS) if g == f] for f in range(F)]
    XU_ROWS, XUZ_ROWS, ALL_ROWS = len(X) + len(U), len(X) + len(U) + len(Z), len(ROWS)
    COLS = SLOTS[U[0]][1] + 1
    UNDER = [(ALL_ROWS, 0, SLOTS[Y[1]][0]), (ALL_ROWS, 3, SLOTS[Z[0]][0])]
    WHOLE = [(ALL_ROWS, 1, SLOTS[X[JB]][0]), (ALL_ROWS, 2, SLOTS[X[2 * JB]][0])]
    OVER = [(XUZ_ROWS, 0, SLOTS[X[0]][0]), (XU_ROWS, 3, SLOTS[Y[0]][0])]
    NVEC = M1 + 2 * M2

    SMALL = [f for f in range(F) if tables[f].shape[0] <= 8 * P]
    HOT = sorted(SMALL[-HOT_MOST:], key=lambda f: f not in U)
    NH = len(HOT)
    VH = tables[HOT[0]].shape[0]
    KT = -(-VH // P)
    VP = VH // KT
    assert VP * KT == VH and all(tables[f].shape[0] == VH for f in HOT)

    GROUPS = [list(range(f, min(f + FG, a + n))) for a, n in runs([f for f in range(F) if f not in HOT])
              for f in range(a, a + n, FG)]
    GROUPS[-1:] = [GROUPS[-1][:-1], GROUPS[-1][-1:]]
    NG = len(GROUPS)
    AFTER_GRAM, MID_LAYER1, LATE_LAYER1, AFTER_LAYER1, MID_LAYER2, AFTER_LAYER2 = (
        range(0, 2), range(2, 3), range(3, 4), range(4, NG - 2), range(NG - 2, NG - 1), range(NG - 1, NG))

    NBANK = [len(range(k, NG, 2)) for k in range(2)]

    def gathered_after(h):
        return sum(sum(map(len, GROUPS[:g + 1])) <= 6 + 4 * h for g in range(NG)) if h < NH - 1 else NG

    def first_tile_groups(h):
        return range(gathered_after(h - 1) if h > 0 else 0, gathered_after(h))

    CHUNK = 8
    CHUNKS = QUAD // CHUNK
    EARLY, LATE = range(0, 2), range(2, CHUNKS)
    GW = P
    assert M1 == 4 and M2 == 2 and D == P and B % P == 0 and F <= QUAD and W1_in.shape[0] == 2 * D + NPAIR
    assert NQ * COLS <= GW and ALL_ROWS <= QUAD

    with ExitStack() as ctx:
        def sb(name, shape, dt=F32):
            return ctx.enter_context(nc.sbuf_tensor(name, shape, dt))

        def psum(name, shape):
            return ctx.enter_context(nc.psum_tensor(name, shape, F32))

        def sem(name):
            return ctx.enter_context(nc.semaphore(name))

        ids = sb("ids", [P, (TILES + 1) * F], I32)
        ids_now = sb("ids_now", [P, F], I32)
        ids_float = sb("ids_float", [P, TILES, F])
        idsT = sb("idsT", [F, TILES * P], F32R)
        pick = sb("pick", [F, NH, P], F32R)
        hot_ids = sb("hot_ids", [P, NH, TILES * P])
        row_ints = sb("row_ints", [P, KT], I32)
        row_number = sb("row_number", [P, KT])
        minus_row = sb("minus_row", [P, 1])
        one = sb("one", [P, 1])
        distance = sb("distance", [P, TILES * P])
        table_raw = sb("table_raw", [P, 2, KT * D])
        table_hi = sb("table_hi", [P, 2, KT * D], F32R)
        table_lo = sb("table_lo", [P, 2, KT * D], F32R)
        onehot = sb("onehot", [P, 2, KT, TILES * P], F32R)
        found = sb("found", [P, NH, TILES * P])
        rows = sb("rows", [P, F - NH, D])
        embed = sb("embed", [P, QUAD, NQ, QUAD])
        pairs = sb("pairs", [P, JB, P])
        bottom = sb("bottom", [P, TILES, D])
        bottomT = sb("bottomT", [P, TILES * P])
        ident = sb("ident", [P, P])
        w_pairs = sb("w_pairs", [P, JB, H1])
        w_bot = sb("w_bot", [P, 2, H1])
        w_bottom = sb("w_bottom", [P, H1])
        w2 = sb("w2", [P, M1, H2])
        vec_rows = sb("vec_rows", [NVEC, P])
        vecs = sb("vecs", [P, NVEC])
        b1, b2, w3 = vecs[:, 0:M1], vecs[:, M1:M1 + M2], vecs[:, M1 + M2:]
        h1 = sb("h1", [P, M1, P])
        h2 = sb("h2", [P, M2, P])
        y = sb("y", [1, B])

        turned = [psum(f"turned{k}", [P, FG, P]) for k in range(2)]
        gram = [psum(f"gram{k}", [P, CHUNK * GW]) for k in range(2)]
        h1_ps = [psum(f"h1_ps{k}", [P, 4 * P]) for k in range(2)]
        y_ps = h1_ps[1][0:1, P:2 * P]
        bottom_ps, idsT_ps, vecs_ps = h1_ps[0], h1_ps[1], h1_ps[1][:, 0:NVEC]
        found_ps = [gram[(h + NH) % 2][:, 0:TILES * P] for h in range(2)]
        hot_ids_ps = [gram[k][:, 4 * P:4 * P + TILES * P] for k in range(2)]

        ids_loaded = sem("ids_loaded")
        bottom_loaded = sem("bottom_loaded")
        w_bot_loaded = sem("w_bot_loaded")
        w_pairs_loaded = sem("w_pairs_loaded")
        w2_loaded = sem("w2_loaded")
        vecs_loaded = sem("vecs_loaded")
        table_loaded = [sem(f"table_loaded{h}") for h in range(NH)]
        gathered = [sem(f"gathered{f}") for f in range(F)]
        ids_padded = sem("ids_padded")
        ids_staged = sem("ids_staged")
        group_started = sem("group_started")
        w_zeroed = sem("w_zeroed")
        ident_zeroed = sem("ident_zeroed")
        ident_ready = sem("ident_ready")
        rows_counted = sem("rows_counted")
        zeros_set = sem("zeros_set")
        ids_floated = sem("ids_floated")
        row_number_set = sem("row_number_set")
        idsT_turned = sem("idsT_turned")
        idsT_ready = sem("idsT_ready")
        pick_ready = sem("pick_ready")
        hot_ids_spread = sem("hot_ids_spread")
        hot_ids_ready = sem("hot_ids_ready")
        table_hi_ready = sem("table_hi_ready")
        table_split = sem("table_split")
        onehot_ready = sem("onehot_ready")
        minus_row_set = sem("minus_row_set")
        distance_ready = sem("distance_ready")
        onehot_by_act = sem("onehot_by_act")
        hot_summed = sem("hot_summed")
        found_ready = sem("found_ready")
        w_bottom_ready = sem("w_bottom_ready")
        bottom_turned = sem("bottom_turned")
        bottomT_ready = sem("bottomT_ready")
        vecs_turned = sem("vecs_turned")
        vecs_ready = sem("vecs_ready")
        group_turned = sem("group_turned")
        bank_copied = [sem(f"bank{k}_copied") for k in range(2)]
        hot_by_act = sem("hot_by_act")
        hot_by_dve = sem("hot_by_dve")
        gram_ready = sem("gram_ready")
        under_by_dve = sem("under_by_dve")
        under_by_act = sem("under_by_act")
        pairs_by_dve = sem("pairs_by_dve")
        pairs_by_act = sem("pairs_by_act")
        h1_summed = sem("h1_summed")
        h1_by_dve = sem("h1_by_dve")
        h1_by_act = sem("h1_by_act")
        h2_summed = sem("h2_summed")
        h2_by_dve = sem("h2_by_dve")
        h2_by_act = sem("h2_by_act")
        y_summed = sem("y_summed")
        y_ready = sem("y_ready")
        y_stored = sem("y_stored")

        block = ctx.enter_context(nc.Block())

        cold_slot = {f: k for k, f in enumerate(f for g in GROUPS for f in g)}

        def h1_part(m):
            k = 0 if m == M1 - 1 else m // (M1 // 2)
            c = M1 // 2 if m == M1 - 1 else m % (M1 // 2)
            return h1_ps[k][:, c * P:(c + 1) * P]

        def h2_half(m):
            return gram[m // (M2 // 2)][:, (m % (M2 // 2)) * P:(m % (M2 // 2) + 1) * P]

        def copy_features(copy, first, n, src):
            while n:
                f = first
                if f in U:
                    k, (a, b) = 1, SLOTS[f]
                    dst, taken = embed[:, :, :, a:b + 1:b - a], src[:, 0:1, :].broadcast_to([P, 2, P])
                else:
                    k = next(k for k in range(1, n + 1) if k == n or SLOTS[f + k][0] != SLOTS[f][0] + k)
                    dst, taken = embed[:, :, :, SLOTS[f][0]:SLOTS[f][0] + k], src[:, 0:k, :]
                last = copy(dst.rearrange("d g q f -> d q g f"), taken.rearrange("d f (q g) -> d q g f", q=NQ))
                first, n, src = first + k, n - k, (src[:, k:, :] if k < n else None)
            return last

        def copy_group(copy, g):
            return copy_features(copy, GROUPS[g][0], len(GROUPS[g]), turned[g % 2][:, 0:len(GROUPS[g]), :])

        def copy_pairs(copy, c, quarters, parts):
            for n_rows, lane, col in parts:
                for q in quarters:
                    own = gram[c % 2][q * QUAD:q * QUAD + n_rows, :].rearrange("i (g c) -> i c g", c=GW)
                    s0 = q * QUAD + c * CHUNK
                    last = copy(pairs[lane * QUAD:lane * QUAD + n_rows, :, s0:s0 + CHUNK],
                                own[:, q * COLS + col:q * COLS + col + JB, :])
            return last

        def pair_weights():
            def pair(i, c):
                return D + c * (c - 1) // 2 + i

            for c in X:
                lane, jb = divmod(c - X[0], JB)
                yield lane * QUAD + SLOTS[Z[0]][0], len(Z), jb, 1, pair(Z[0], c)
                if c > X[0]:
                    yield lane * QUAD, c - X[0], jb, 1, pair(X[0], c)
            for u in U:
                for lane in range(NQ):
                    yield lane * QUAD + SLOTS[u][0], 1, 0, JB, pair(X[lane * JB] if lane < 3 else Y[0], u)
            for jb, c in enumerate(Y):
                yield 3 * QUAD, len(X), jb, 1, pair(X[0], c)
            for r in (*Y, *U):
                yield 3 * QUAD + SLOTS[r][-1], 1, 0, JB, pair(Z[0], r)
            for c in Z[1:]:
                yield 3 * QUAD + SLOTS[Z[0]][0], c - Z[0], c - Z[0], 1, pair(Z[0], c)
            for c in Y[1:]:
                yield SLOTS[Y[0]][0], c - Y[0], c - Y[1], 1, pair(Y[0], c)
            yield SLOTS[U[1]][1], 1, JB - 1, 1, pair(U[0], U[1])

        WEIGHTS = list(pair_weights())

        @block.sync
        def _(sp):
            sp.dma_start(ids[:, 0:TILES * F], ids_in.rearrange("(p t) f -> p (t f)", t=TILES)).then_inc(ids_loaded, 16)

            def load_table(h):
                src = tables[HOT[h]].rearrange("(p k) d -> p (k d)", k=KT)
                for a, b in ((0, VP // 16 * 16), (VP // 16 * 16, VP)):
                    sp.dma_start(table_raw[a:b, h % 2, :], src[a:b, :]).then_inc(table_loaded[h], 16)

            load_table(0)
            sp.dma_start(bottom[:, :, :], bottom_in.rearrange("(p t) d -> p t d", t=TILES)).then_inc(bottom_loaded, 16)
            load_table(1)
            sp.dma_start(vec_rows[0:M1, :], b1_in.rearrange("(m p) -> m p", p=P)).then_inc(vecs_loaded, 16)
            sp.dma_start(vec_rows[M1:M1 + M2, :], b2_in.rearrange("(m p) -> m p", p=P)).then_inc(vecs_loaded, 16)
            sp.dma_start(vec_rows[M1 + M2:, :], W3_in.rearrange("(m p) o -> m (p o)", p=P)).then_inc(vecs_loaded, 16)
            weights = iter(WEIGHTS)

            def load_weights(n):
                for p0, rows_, jb, tiles_, r0 in islice(weights, n):
                    sp.dma_start(w_pairs[p0:p0 + rows_, jb:jb + tiles_, :],
                                 W1_in[r0:r0 + rows_ * tiles_, :].rearrange("(r j) n -> r j n", j=tiles_)
                                 ).then_inc(w_pairs_loaded, 16)

            sp.wait_ge(w_zeroed, 2)
            load_weights(4)
            for h in range(2, NH):
                sp.wait_ge(table_split, h - 1)
                load_table(h)
                if h == NH - 1:
                    sp.dma_start(w_bot[:, 0, :], W1_in[0:D, :]).then_inc(w_bot_loaded, 16)
                    sp.dma_start(w_bot[:, 1, :], W1_in[D + NPAIR:, :]).then_inc(w_bot_loaded, 16)
                load_weights(7)
            load_weights(len(WEIGHTS))
            sp.dma_start(w2[:, :, :], W2_in.rearrange("(m p) n -> p m n", p=P)).then_inc(w2_loaded, 16)
            sp.wait_ge(y_ready, TILES + 1)
            sp.dma_start(out.rearrange("b o -> o b"), y[:, :]).then_inc(y_stored, 16)
            sp.wait_ge(y_stored, 16)

        @block.gpsimd
        def _(pool):
            pool.memset(ident[:, :], 0.0).then_inc(ident_zeroed, 1)
            pool.wait_ge(ident_zeroed, 1)
            pool.affine_select(out=ident[:, :], in_=ident[:, :], compare_op=ALU.not_equal, fill=1.0,
                               base=0, pattern=[[-1, P]], channel_multiplier=1).then_inc(ident_ready, 1)
            pool.iota(row_ints[:, :], [[1, KT]], 0, KT).then_inc(rows_counted, 1)
            pool.memset(w_pairs[:, 2:, :], 0.0).then_inc(w_zeroed, 1)

            def gather(group, tile_ids):
                for f in group:
                    pool.indirect_dma_start(
                        out=rows[:, cold_slot[f], :], out_offset=None, in_=tables[f],
                        in_offset=bass.IndirectOffsetOnAxis(ap=tile_ids[:, f:f + 1], axis=0),
                    ).then_inc(gathered[f], 16)

            pool.wait_ge(ids_loaded, 16)
            for group in GROUPS:
                gather(group, ids)
            with pool.Fori(0, LAST) as t:
                for n, group in enumerate(GROUPS):
                    pool.wait_ge(ids_staged, t * NG + n + 1)
                    pool.sem_inc(group_started, 1)
                    gather(group, ids_now)

        @block.tensor
        def _(pe):
            pe.wait_ge(ident_ready, 1)

            def warm_up(n):
                for _ in range(n):
                    pe.transpose(turned[1][:, 0, :], ident[:, :], ident[:, :])

            warm_up(9)
            pe.wait_ge(ids_floated, 1)
            for t in range(TILES):
                last = pe.transpose(idsT_ps[0:F, t * P:(t + 1) * P], ids_float[:, t, :], ident[:, :])
            last.then_inc(idsT_turned, 1)
            warm_up(5)
            pe.wait_ge(idsT_ready, 1)
            pe.wait_ge(pick_ready, 1)

            def spread_ids(h):
                if h >= 2:
                    pe.wait_ge(hot_ids_ready, h - 1)
                pe.matmul(hot_ids_ps[h % 2], pick[:, h, :], idsT[:, :], start=True, stop=True).then_inc(hot_ids_spread, 1)

            spread_ids(0)
            spread_ids(1)
            def turn_bottom():
                pe.wait_ge(bottom_loaded, 16)
                for t in range(TILES):
                    last = pe.transpose(bottom_ps[:, t * P:(t + 1) * P], bottom[:, t, :], ident[:, :])
                last.then_inc(bottom_turned, 1)

            def turn_vecs():
                pe.wait_ge(vecs_loaded, 48)
                pe.transpose(vecs_ps, vec_rows[:, :], ident[0:NVEC, 0:NVEC]).then_inc(vecs_turned, 1)

            def turn(t, groups, first=False):
                for g in groups or ():
                    if not (first and g < 2):
                        pe.wait_ge(bank_copied[g % 2], t * NBANK[g % 2] + g // 2)
                    for k, f in enumerate(GROUPS[g]):
                        pe.wait_ge(gathered[f], (t + 1) * 16)
                        last = pe.transpose(turned[g % 2][:, k, :], rows[:, cold_slot[f], :], ident[:, :])
                    last.then_inc(group_turned, 1)

            def look_up(h):
                pe.wait_ge(table_split, h + 1)
                if h >= 2:
                    pe.wait_ge(found_ready, h - 1)
                for kt in range(KT):
                    if kt < KT - 1:
                        pe.wait_ge(onehot_ready, h * (KT - 1) + kt + 1)
                    else:
                        pe.wait_ge(onehot_by_act, h + 1)
                    for part in (table_hi, table_lo):
                        last = pe.matmul(found_ps[h % 2], part[0:VP, h % 2, kt * D:(kt + 1) * D],
                                         onehot[0:VP, h % 2, kt, :], start=(kt == 0 and part is table_hi),
                                         stop=(kt == KT - 1 and part is table_lo))
                last.then_inc(hot_summed, 1)

            def grams(t, chunks):
                for c in chunks:
                    if c >= 2:
                        pe.wait_ge(pairs_by_dve, t * CHUNKS + c - 1)
                        pe.wait_ge(pairs_by_act, t * CHUNKS + c - 1)
                    for g in range(CHUNK):
                        four = embed[:, c * CHUNK + g, :, :]
                        last = pe.matmul(gram[c % 2][:, g * GW:g * GW + NQ * COLS],
                                         four, four[:, :, 0:COLS], start=True, stop=True)
                    last.then_inc(gram_ready, 1)

            def layer1_bottom(t):
                for m in range(M1):
                    pe.matmul(h1_part(m), w_bottom[:, m * P:(m + 1) * P], bottomT[:, bass.ds(t * P, P)],
                              start=(m % (M1 // 2) == 0), stop=False, skip_group_check=True)

            def layer1_pairs(m):
                for jb in range(JB):
                    last = pe.matmul(h1_part(m), w_pairs[:, jb, m * P:(m + 1) * P], pairs[:, jb, :],
                                     start=False, stop=(jb == JB - 1), skip_group_check=True)
                last.then_inc(h1_summed, 1)

            def layer2(m, ks):
                for k in ks:
                    last = pe.matmul(h2_half(m), w2[:, k, m * P:(m + 1) * P], h1[:, k, :],
                                     start=(k == 0), stop=(k == M1 - 1))
                return last

            def layer3(t):
                for k in range(M2):
                    pe.wait_ge(h2_by_act if k else h2_by_dve, t + 1)
                    last = pe.matmul(y_ps, w3[:, k:k + 1], h2[:, k, :], start=(k == 0), stop=(k == M2 - 1))
                last.then_inc(y_summed, 1)

            def tile(t, turns):
                grams(t, LATE)
                turn(t + 1, turns and AFTER_GRAM)
                pe.wait_ge(y_ready, t + 1)
                layer1_bottom(t)
                pe.wait_ge(w_pairs_loaded, 16 * len(WEIGHTS))
                pe.wait_ge(w2_loaded, 16)
                pe.wait_ge(pairs_by_dve, (t + 1) * CHUNKS)
                pe.wait_ge(pairs_by_act, (t + 1) * CHUNKS)
                layer1_pairs(0)
                layer1_pairs(1)
                turn(t + 1, turns and MID_LAYER1)
                layer1_pairs(2)
                turn(t + 1, turns and LATE_LAYER1)
                pe.wait_ge(h1_by_dve, 3 * t + 2)
                layer1_pairs(3)
                turn(t + 1, turns and AFTER_LAYER1)
                pe.wait_ge(h1_by_act, t + 1)
                layer2(0, range(M1 - 1))
                pe.wait_ge(h1_by_dve, 3 * t + 3)
                layer2(0, range(M1 - 1, M1)).then_inc(h2_summed, 1)
                turn(t + 1, turns and MID_LAYER2)
                layer2(1, range(M1)).then_inc(h2_summed, 1)
                turn(t + 1, turns and AFTER_LAYER2)
                if turns:
                    pe.wait_ge(hot_by_act, t + 2)
                    for k in range(2):
                        pe.wait_ge(bank_copied[k], (t + 2) * NBANK[k])
                    pe.wait_ge(h2_by_dve, t + 1)
                    grams(t + 1, EARLY[:1])
                    pe.wait_ge(h2_by_act, t + 1)
                    grams(t + 1, EARLY[1:])
                layer3(t)

            turn_bottom()
            turn_vecs()
            for h in range(NH):
                if h + 2 < NH:
                    spread_ids(h + 2)
                look_up(h)
                turn(0, first_tile_groups(h), True)
            pe.wait_ge(hot_by_act, 1)
            pe.wait_ge(hot_by_dve, 1)
            for k in range(2):
                pe.wait_ge(bank_copied[k], NBANK[k])
            pe.wait_ge(found_ready, NH - 1)
            grams(0, EARLY[:1])
            pe.wait_ge(found_ready, NH)
            grams(0, EARLY[1:])
            pe.wait_ge(bottomT_ready, 1)
            pe.wait_ge(zeros_set, 2)
            pe.wait_ge(w_bottom_ready, 1)
            with pe.Fori(0, LAST) as t:
                tile(t, True)
            tile(LAST, False)

        @block.vector
        def _(dve):
            def stage_ids(t, n):
                f, count = GROUPS[n][0], len(GROUPS[n])
                dve.tensor_copy(ids_now[:, f:f + count], ids[:, bass.ds(t * F + f, count)]).then_inc(ids_staged, 1)

            def split_table(h):
                dve.wait_ge(table_hi_ready, h + 1)
                if h >= 2:
                    dve.wait_ge(hot_summed, h - 1)
                dve.tensor_tensor(table_lo[0:VP, h % 2, :], table_raw[0:VP, h % 2, :], table_hi[0:VP, h % 2, :],
                                  ALU.subtract).then_inc(table_split, 1)

            def make_onehot(h):
                dve.wait_ge(hot_ids_ready, h + 1)
                for kt in range(KT - 1):
                    dve.tensor_scalar(onehot[0:VP, h % 2, kt, :], hot_ids[0:VP, h, :],
                                      row_number[0:VP, kt:kt + 1], None, ALU.is_equal).then_inc(onehot_ready, 1)

            def groups(t, which, copy=True):
                for g in which or ():
                    dve.wait_ge(group_turned, t * NG + g + 1)
                    stage_ids(t + 1, g)
                    if copy and g % 2 == 0:
                        copy_group(dve.tensor_copy, g).then_inc(bank_copied[0], 1)

            def relu1(t, ms):
                for m in ms:
                    dve.wait_ge(h1_summed, M1 * t + max(m + 1, 2))
                    dve.tensor_scalar(h1[:, m, :], h1_part(m), b1[:, m:m + 1], 0.0, ALU.add, ALU.max).then_inc(h1_by_dve, 1)

            def relu2(t):
                dve.wait_ge(h2_summed, t * M2 + 1)
                for m in range(M2 // 2):
                    last = dve.tensor_scalar(h2[:, m, :], h2_half(m), b2[:, m:m + 1], 0.0, ALU.add, ALU.max)
                last.then_inc(h2_by_dve, 1)

            dve.memset(ids[:, TILES * F:], 0).then_inc(ids_padded, 1)
            dve.memset(w_pairs[:, 0:2, :], 0.0).then_inc(w_zeroed, 1)
            dve.memset(pairs[:, :, :], 0.0).then_inc(zeros_set, 1)
            dve.wait_ge(rows_counted, 1)
            dve.tensor_copy(row_number[:, :], row_ints[:, :]).then_inc(row_number_set, 1)
            dve.tensor_scalar(minus_row[:, :], row_ints[:, KT - 1:KT], -1.0, None, ALU.mult).then_inc(minus_row_set, 1)
            dve.memset(one[:, :], 1.0).then_inc(minus_row_set, 1)
            dve.wait_ge(ids_padded, 1)
            dve.wait_ge(ids_loaded, 16)
            dve.tensor_copy(ids_float[:, :, :].rearrange("p t f -> p (t f)"), ids[:, 0:TILES * F]).then_inc(ids_floated, 1)
            dve.memset(embed[:, :, :, ALL_ROWS:], 0.0).then_inc(zeros_set, 1)
            dve.wait_ge(idsT_turned, 1)
            dve.tensor_copy(idsT[:, :], idsT_ps[0:F, :]).then_inc(idsT_ready, 1)
            dve.wait_ge(row_number_set, 1)
            for h in range(NH):
                split_table(h)
                make_onehot(h)
                if h == 0:
                    dve.wait_ge(zeros_set, 2)
                else:
                    groups(0, first_tile_groups(h - 1), False)
            groups(0, first_tile_groups(NH - 1), False)
            dve.wait_ge(w_bot_loaded, 32)
            dve.tensor_tensor(w_bottom[:, :], w_bot[:, 0, :], w_bot[:, 1, :], ALU.add).then_inc(w_bottom_ready, 1)
            dve.wait_ge(hot_summed, NH)
            copy_features(dve.tensor_copy, HOT[-1], 1,
                          found_ps[(NH - 1) % 2][:, 0:P].rearrange("d (f s) -> d f s", f=1)).then_inc(hot_by_dve, 1)
            dve.wait_ge(vecs_ready, 1)

            def tile(t, turns):
                for c in range(CHUNKS):
                    dve.wait_ge(gram_ready, t * CHUNKS + c + 1)
                    copy_pairs(dve.tensor_copy, c, range(NQ // 2), UNDER).then_inc(under_by_dve, 1)
                    copy_pairs(dve.tensor_copy, c, range(NQ // 2), WHOLE)
                    dve.wait_ge(under_by_dve, t * CHUNKS + c + 1)
                    copy_pairs(dve.tensor_copy, c, range(NQ // 2), OVER).then_inc(pairs_by_dve, 1)
                groups(t + 1, turns and AFTER_GRAM)
                relu1(t, (0, 1))
                groups(t + 1, turns and MID_LAYER1)
                groups(t + 1, turns and LATE_LAYER1)
                relu1(t, (3,))
                groups(t + 1, turns and AFTER_LAYER1)
                relu2(t)
                groups(t + 1, turns and MID_LAYER2)
                groups(t + 1, turns and AFTER_LAYER2)

            with dve.Fori(0, LAST) as t:
                tile(t, True)
            tile(LAST, False)

        @block.scalar
        def _(act):
            def groups(t, which, alone=False):
                for g in which or ():
                    if alone or g % 2 == 1:
                        act.wait_ge(group_turned, t * NG + g + 1)
                        copy_group(act.copy, g).then_inc(bank_copied[g % 2], 1)

            def copy_hot(t, features):
                for f, n in runs(features):
                    h = HOT.index(f)
                    last = copy_features(act.copy, f, n, found[:, h:h + n, bass.ds(t * P, P)])
                return last

            def relu1(t):
                act.wait_ge(h1_summed, M1 * t + 3)
                act.activation(h1[:, 2, :], h1_part(2), ACT.Relu, bias=b1[:, 2:3]).then_inc(h1_by_act, 1)

            def relu2(t):
                act.wait_ge(h2_summed, t * M2 + 2)
                for m in range(M2 // 2, M2):
                    last = act.activation(h2[:, m, :], h2_half(m), ACT.Relu, bias=b2[:, m:m + 1])
                last.then_inc(h2_by_act, 1)

            def take_y(t):
                act.wait_ge(y_summed, t + 1)
                act.copy(y[0:1, bass.ds(t, P, TILES)], y_ps).then_inc(y_ready, 1)

            act.wait_ge(ident_ready, 1)
            for h, f in enumerate(HOT):
                last = act.copy(pick[:, h, :], ident[0:F, f:f + 1].broadcast_to([F, P]))
            last.then_inc(pick_ready, 1)

            def take_ids(h):
                act.wait_ge(hot_ids_spread, h + 1)
                act.copy(hot_ids[:, h, :], hot_ids_ps[h % 2]).then_inc(hot_ids_ready, 1)

            def take_hi(h):
                act.wait_ge(table_loaded[h], 32)
                act.copy(table_hi[0:VP, h % 2, :], table_raw[0:VP, h % 2, :]).then_inc(table_hi_ready, 1)

            def make_onehot(h):
                act.wait_ge(hot_ids_ready, h + 1)
                if h > 0:
                    act.wait_ge(onehot_by_act, h)
                act.activation(distance[0:VP, :], hot_ids[0:VP, h, :], ACT.Square,
                               bias=minus_row[0:VP, :]).then_inc(distance_ready, 1)
                act.wait_ge(distance_ready, h + 1)
                if h >= 2:
                    act.wait_ge(hot_summed, h - 1)
                act.activation(onehot[0:VP, h % 2, KT - 1, :], distance[0:VP, :], ACT.Relu,
                               bias=one[0:VP, :], scale=-1.0).then_inc(onehot_by_act, 1)

            take_hi(0)
            take_ids(0)
            take_ids(1)
            take_hi(1)
            act.wait_ge(minus_row_set, 2)
            make_onehot(0)
            act.wait_ge(zeros_set, 2)
            for h in range(NH):
                if h + 2 < NH:
                    take_ids(h + 2)
                if h + 1 < NH:
                    make_onehot(h + 1)
                if h > 0:
                    act.wait_ge(found_ready, h)
                    last = copy_hot(0, HOT[h - 1:h])
                    if h == NH - 1:
                        last.then_inc(hot_by_act, 1)
                act.wait_ge(hot_summed, h + 1)
                if h == NH - 1:
                    act.wait_ge(hot_by_dve, 1)
                act.copy(found[:, h, :], found_ps[h % 2]).then_inc(found_ready, 1)
                if h == 0:
                    act.wait_ge(vecs_turned, 1)
                    act.copy(vecs[:, :], vecs_ps).then_inc(vecs_ready, 1)
                    act.wait_ge(bottom_turned, 1)
                    act.copy(bottomT[:, :], bottom_ps[:, :]).then_inc(bottomT_ready, 1)
                if h + 2 < NH:
                    take_hi(h + 2)
                groups(0, first_tile_groups(h), True)
            act.wait_ge(vecs_ready, 1)
            act.wait_ge(found_ready, NH)
            act.sem_inc(y_ready, 1)

            def take_pairs(t, chunks):
                for c in chunks:
                    act.wait_ge(gram_ready, t * CHUNKS + c + 1)
                    copy_pairs(act.copy, c, range(NQ // 2, NQ), UNDER).then_inc(under_by_act, 1)
                    copy_pairs(act.copy, c, range(NQ // 2, NQ), WHOLE)
                    act.wait_ge(under_by_act, t * CHUNKS + c + 1)
                    copy_pairs(act.copy, c, range(NQ // 2, NQ), OVER).then_inc(pairs_by_act, 1)

            def tile(t, turns):
                take_pairs(t, LATE)
                groups(t + 1, turns and AFTER_GRAM)
                if turns:
                    copy_hot(t + 1, HOT).then_inc(hot_by_act, 1)
                groups(t + 1, turns and MID_LAYER1)
                relu1(t)
                groups(t + 1, turns and LATE_LAYER1)
                groups(t + 1, turns and AFTER_LAYER1)
                groups(t + 1, turns and MID_LAYER2)
                groups(t + 1, turns and AFTER_LAYER2)
                relu2(t)
                take_pairs(t + 1, turns and EARLY or ())
                take_y(t)

            take_pairs(0, EARLY)
            with act.Fori(0, LAST) as t:
                tile(t, True)
            tile(LAST, False)


def kernel(**inputs):
    import numpy as np
    import concourse.bacc as bacc
    from concourse.bass_utils import run_bass_kernel_spmd as run

    F = inputs["ids"].shape[1]
    names = (["r_bottom_mlp_out", "ids"] + [f"tbl_{f}" for f in range(F)]
             + ["W_top1", "b_top1", "W_top2", "b_top2", "W_top3"])
    nc = bacc.Bacc("TRN2", target_bir_lowering=False, num_devices=1)
    arrays, aps = {}, {}
    for name in names:
        a = np.ascontiguousarray(inputs[name])
        arrays[f"in_{name}"] = a
        aps[name] = nc.dram_tensor(f"in_{name}", a.shape, mybir.dt.from_np(a.dtype), kind="ExternalInput").ap()
    out = nc.dram_tensor("out_y", (inputs["ids"].shape[0], 1), F32, kind="ExternalOutput").ap()
    build_dlrm(nc, aps["r_bottom_mlp_out"], aps["ids"], [aps[f"tbl_{f}"] for f in range(F)],
               aps["W_top1"], aps["b_top1"], aps["W_top2"], aps["b_top2"], aps["W_top3"], out)
    return run(nc, [arrays], core_ids=[0]).results[0]["out_y"]
```
